# Optimizing a Trainium2 kernel written in Bass

```python
import numpy as np
import jax
import jax.numpy as jnp

def _softmax(x, axis=-1):
    return jax.nn.softmax(x, axis=axis)

def _gelu(x):
    return jax.nn.gelu(x, approximate=True)

def _silu(x):
    return jax.nn.silu(x)

def _sigmoid(x):
    return jax.nn.sigmoid(x)

def _layernorm(x, axis=-1, eps=1e-05):
    m = jnp.mean(x, axis=axis, keepdims=True)
    v = jnp.var(x, axis=axis, keepdims=True)
    return (x - m) / jnp.sqrt(v + eps)

def _scatter_add(tgt, idx, src, axis=0):
    return tgt.at[idx].add(src)

def _segment_sum(src, seg, n):
    return jax.ops.segment_sum(src, seg, n)
kernel_name = 'mk_macaron_d2_jaxref_r8_398cfe'

def setup_inputs(seed: int=0):
    np.random.seed(seed)
    _w = jnp.asarray

    def _L0_attn_setup():
        import jax, jax.numpy as jnp
        import numpy as np
        B, S, D = (4, 256, 128)

        def _wkv(k, v, time_decay, u):
            w = -jnp.exp(time_decay)
            b, s, d = k.shape
            aa = jnp.zeros((b, d), k.dtype)
            bb = jnp.zeros((b, d), k.dtype)
            pp = jnp.full((b, d), -1e+30, k.dtype)

            def step(carry, kv):
                aa, bb, pp = carry
                kk, vv = kv
                ww = u + kk
                p = jnp.maximum(pp, ww)
                e1 = jnp.exp(pp - p)
                e2 = jnp.exp(ww - p)
                out = (e1 * aa + e2 * vv) / (e1 * bb + e2)
                ww2 = w + pp
                p2 = jnp.maximum(ww2, kk)
                e1b = jnp.exp(ww2 - p2)
                e2b = jnp.exp(kk - p2)
                return ((e1b * aa + e2b * vv, e1b * bb + e2b, p2), out)
            _, outs = jax.lax.scan(step, (aa, bb, pp), (k.transpose(1, 0, 2), v.transpose(1, 0, 2)))
            return outs.transpose(1, 0, 2)
        key = jax.random.key(seed)
        ks = jax.random.split(key, 10)
        s = 0.02
        return {'x': jax.random.normal(ks[0], (B, S, D), jnp.float32), 'time_mix_k': jax.random.uniform(ks[1], (1, 1, D), jnp.float32), 'time_mix_v': jax.random.uniform(ks[2], (1, 1, D), jnp.float32), 'time_mix_r': jax.random.uniform(ks[3], (1, 1, D), jnp.float32), 'time_decay': jax.random.normal(ks[4], (D,), jnp.float32) * 0.1, 'time_first': jax.random.normal(ks[5], (D,), jnp.float32) * 0.1, 'Wk': jax.random.normal(ks[6], (D, D), jnp.float32) * s, 'Wv': jax.random.normal(ks[7], (D, D), jnp.float32) * s, 'Wr': jax.random.normal(ks[8], (D, D), jnp.float32) * s, 'Wo': jax.random.normal(ks[9], (D, D), jnp.float32) * s}
    _L0_attn_in = _L0_attn_setup()

    def _L0_ffn_setup():
        import jax, jax.numpy as jnp
        import numpy as np
        D, F, E, K = (128, 344, 8, 2)
        key = jax.random.key(seed)
        k0, k1, k2, k3, k4 = jax.random.split(key, 5)
        s = 0.02
        x = jax.random.normal(k0, (2, 64, D), jnp.float32)
        Ws = jax.random.normal(k1, (D, E), jnp.float32) * s
        bs = jnp.zeros((E,), jnp.float32)
        Wg = jax.random.normal(k2, (E, D, F), jnp.float32) * s
        Wu = jax.random.normal(k3, (E, D, F), jnp.float32) * s
        Wd = jax.random.normal(k4, (E, F, D), jnp.float32) * s
        return {'x': x, 'Ws': Ws, 'bs': bs, 'Wg': Wg, 'Wu': Wu, 'Wd': Wd}
    _L0_ffn_in = _L0_ffn_setup()

    def _L1_attn_setup():
        import jax, jax.numpy as jnp
        import numpy as np
        EMBED_DIM = 128
        NUM_HEADS = 16
        HEAD_DIM = EMBED_DIM // NUM_HEADS
        SCALING = HEAD_DIM ** (-0.5)
        EPS = 1e-05

        def _rope(seq_len):
            inv_freq = 1.0 / 10000.0 ** (jnp.arange(0, HEAD_DIM, 2, dtype=jnp.float32) / HEAD_DIM)
            freqs = jnp.arange(seq_len, dtype=jnp.float32)[:, None] * inv_freq[None, :]
            emb = jnp.concatenate([freqs, freqs], axis=-1)
            return (jnp.cos(emb), jnp.sin(emb))

        def _rotate(x, cos, sin):
            d = x.shape[-1]
            x1, x2 = (x[..., :d // 2], x[..., d // 2:])
            rotated = jnp.concatenate([-x2, x1], axis=-1)
            return x * cos + rotated * sin
        key = jax.random.key(seed)
        ks = jax.random.split(key, 6)
        B, S, D = (2, 256, EMBED_DIM)
        scale = D ** (-0.5)
        return {'x': jax.random.normal(ks[0], (B, S, D), jnp.float32), 'Wq': jax.random.normal(ks[1], (D, D), jnp.float32) * scale, 'Wk': jax.random.normal(ks[2], (D, D), jnp.float32) * scale, 'Wv': jax.random.normal(ks[3], (D, D), jnp.float32) * scale, 'Wg': jax.random.normal(ks[4], (D, D), jnp.float32) * scale, 'Wo': jax.random.normal(ks[5], (D, D), jnp.float32) * scale, 'gn_w': jnp.ones((D,), jnp.float32), 'gn_b': jnp.zeros((D,), jnp.float32)}
    _L1_attn_in = _L1_attn_setup()

    def _L1_ffn_setup():
        import jax, jax.numpy as jnp
        import numpy as np
        B, T, D, E, H, K = (2, 256, 128, 8, 512, 2)
        key = jax.random.key(seed)
        ks = jax.random.split(key, 8)
        s = 0.02
        return {'x': jax.random.normal(ks[0], (B, T, D), jnp.float32), 'rw1': jax.random.normal(ks[1], (D, D), jnp.float32) * s, 'rb1': jnp.zeros((D,), jnp.float32), 'rw2': jax.random.normal(ks[2], (D, E), jnp.float32) * s, 'rb2': jnp.zeros((E,), jnp.float32), 'we1': jax.random.normal(ks[3], (E, D, H), jnp.float32) * s, 'be1': jnp.zeros((E, H), jnp.float32), 'we2': jax.random.normal(ks[4], (E, H, D), jnp.float32) * s, 'be2': jnp.zeros((E, D), jnp.float32)}
    _L1_ffn_in = _L1_ffn_setup()
    _d = {'L0_attn_x': _L0_attn_in['x'], 'L0_attn_time_mix_k': _L0_attn_in['time_mix_k'], 'L0_attn_time_mix_v': _L0_attn_in['time_mix_v'], 'L0_attn_time_mix_r': _L0_attn_in['time_mix_r'], 'L0_attn_time_decay': _L0_attn_in['time_decay'], 'L0_attn_time_first': _L0_attn_in['time_first'], 'L0_attn_Wk': _L0_attn_in['Wk'], 'L0_attn_Wv': _L0_attn_in['Wv'], 'L0_attn_Wr': _L0_attn_in['Wr'], 'L0_attn_Wo': _L0_attn_in['Wo'], 'L0_ffn_Ws': _L0_ffn_in['Ws'], 'L0_ffn_bs': _L0_ffn_in['bs'], 'L0_ffn_Wg': _L0_ffn_in['Wg'], 'L0_ffn_Wu': _L0_ffn_in['Wu'], 'L0_ffn_Wd': _L0_ffn_in['Wd'], 'L1_attn_Wq': _L1_attn_in['Wq'], 'L1_attn_Wk': _L1_attn_in['Wk'], 'L1_attn_Wv': _L1_attn_in['Wv'], 'L1_attn_Wg': _L1_attn_in['Wg'], 'L1_attn_Wo': _L1_attn_in['Wo'], 'L1_attn_gn_w': _L1_attn_in['gn_w'], 'L1_attn_gn_b': _L1_attn_in['gn_b'], 'L1_ffn_rw1': _L1_ffn_in['rw1'], 'L1_ffn_rb1': _L1_ffn_in['rb1'], 'L1_ffn_rw2': _L1_ffn_in['rw2'], 'L1_ffn_rb2': _L1_ffn_in['rb2'], 'L1_ffn_we1': _L1_ffn_in['we1'], 'L1_ffn_be1': _L1_ffn_in['be1'], 'L1_ffn_we2': _L1_ffn_in['we2'], 'L1_ffn_be2': _L1_ffn_in['be2']}
    _x0 = _d['L0_attn_x']
    _d['L0_attn_x'] = jax.random.normal(jax.random.fold_in(jax.random.key(seed), 1), (2, 1024, 128), dtype=_x0.dtype)
    del _x0
    return _d

def reference(L0_attn_x, L0_attn_time_mix_k, L0_attn_time_mix_v, L0_attn_time_mix_r, L0_attn_time_decay, L0_attn_time_first, L0_attn_Wk, L0_attn_Wv, L0_attn_Wr, L0_attn_Wo, L0_ffn_Ws, L0_ffn_bs, L0_ffn_Wg, L0_ffn_Wu, L0_ffn_Wd, L1_attn_Wq, L1_attn_Wk, L1_attn_Wv, L1_attn_Wg, L1_attn_Wo, L1_attn_gn_w, L1_attn_gn_b, L1_ffn_rw1, L1_ffn_rb1, L1_ffn_rw2, L1_ffn_rb2, L1_ffn_we1, L1_ffn_be1, L1_ffn_we2, L1_ffn_be2):

    def _L0_attn_ref(x, time_mix_k, time_mix_v, time_mix_r, time_decay, time_first, Wk, Wv, Wr, Wo):
        import jax, jax.numpy as jnp
        import numpy as np
        B, S, D = (4, 256, 128)

        def _wkv(k, v, time_decay, u):
            w = -jnp.exp(time_decay)
            b, s, d = k.shape
            aa = jnp.zeros((b, d), k.dtype)
            bb = jnp.zeros((b, d), k.dtype)
            pp = jnp.full((b, d), -1e+30, k.dtype)

            def step(carry, kv):
                aa, bb, pp = carry
                kk, vv = kv
                ww = u + kk
                p = jnp.maximum(pp, ww)
                e1 = jnp.exp(pp - p)
                e2 = jnp.exp(ww - p)
                out = (e1 * aa + e2 * vv) / (e1 * bb + e2)
                ww2 = w + pp
                p2 = jnp.maximum(ww2, kk)
                e1b = jnp.exp(ww2 - p2)
                e2b = jnp.exp(kk - p2)
                return ((e1b * aa + e2b * vv, e1b * bb + e2b, p2), out)
            _, outs = jax.lax.scan(step, (aa, bb, pp), (k.transpose(1, 0, 2), v.transpose(1, 0, 2)))
            return outs.transpose(1, 0, 2)
        shifted = jnp.concatenate([jnp.zeros_like(x[:, :1, :]), x[:, :-1, :]], axis=1)
        xk = x * time_mix_k + shifted * (1.0 - time_mix_k)
        xv = x * time_mix_v + shifted * (1.0 - time_mix_v)
        xr = x * time_mix_r + shifted * (1.0 - time_mix_r)
        k = jnp.einsum('bsd,ed->bse', xk, Wk)
        v = jnp.einsum('bsd,ed->bse', xv, Wv)
        r = jax.nn.sigmoid(jnp.einsum('bsd,ed->bse', xr, Wr))
        wkv = _wkv(k, v, time_decay, time_first)
        out = jnp.einsum('bsd,ed->bse', r * wkv, Wo)
        return out

    def _L0_ffn_ref(x, Ws, bs, Wg, Wu, Wd):
        import jax, jax.numpy as jnp
        import numpy as np
        D, F, E, K = (128, 344, 8, 2)
        b, n, d = x.shape
        xt = x.reshape(-1, d)
        logits = xt @ Ws + bs
        topk_w, topk_idx = jax.lax.top_k(logits, K)
        topk_w = jax.nn.softmax(topk_w, axis=-1)
        combine = jnp.sum(jax.nn.one_hot(topk_idx, E, dtype=xt.dtype) * topk_w[..., None], axis=1)
        g = jnp.einsum('td,edf->tef', xt, Wg)
        u = jnp.einsum('td,edf->tef', xt, Wu)
        h = jax.nn.silu(g) * u
        y = jnp.einsum('tef,efd->ted', h, Wd)
        out = jnp.einsum('ted,te->td', y, combine)
        return out.reshape(b, n, d)

    def _L1_attn_ref(x, Wq, Wk, Wv, Wg, Wo, gn_w, gn_b):
        import jax, jax.numpy as jnp
        import numpy as np
        EMBED_DIM = 128
        NUM_HEADS = 16
        HEAD_DIM = EMBED_DIM // NUM_HEADS
        SCALING = HEAD_DIM ** (-0.5)
        EPS = 1e-05

        def _rope(seq_len):
            inv_freq = 1.0 / 10000.0 ** (jnp.arange(0, HEAD_DIM, 2, dtype=jnp.float32) / HEAD_DIM)
            freqs = jnp.arange(seq_len, dtype=jnp.float32)[:, None] * inv_freq[None, :]
            emb = jnp.concatenate([freqs, freqs], axis=-1)
            return (jnp.cos(emb), jnp.sin(emb))

        def _rotate(x, cos, sin):
            d = x.shape[-1]
            x1, x2 = (x[..., :d // 2], x[..., d // 2:])
            rotated = jnp.concatenate([-x2, x1], axis=-1)
            return x * cos + rotated * sin
        B, S, D = x.shape
        H, Dh = (NUM_HEADS, HEAD_DIM)

        def split_heads(t):
            return t.reshape(B, S, H, Dh).transpose(0, 2, 1, 3)
        q = split_heads(x @ Wq.T)
        k = split_heads(x @ Wk.T)
        v = split_heads(x @ Wv.T)
        cos, sin = _rope(S)
        q = _rotate(q, cos, sin)
        k = _rotate(k, cos, sin)
        retention = jnp.einsum('bhsd,bhtd->bhst', q, k) * SCALING
        gammas = 1.0 - 2.0 ** (-5.0 - jnp.arange(H, dtype=jnp.float32))
        diff = jnp.arange(S)[:, None] - jnp.arange(S)[None, :]
        causal = diff >= 0
        decay = jnp.where(causal, gammas[:, None, None] ** jnp.maximum(diff, 0).astype(jnp.float32), 0.0)
        retention = retention * decay[None]
        out = jnp.einsum('bhst,bhtd->bhsd', retention, v)
        out = out.transpose(0, 2, 1, 3).reshape(B * S, H, Dh)
        mean = out.mean(axis=-1, keepdims=True)
        var = out.var(axis=-1, keepdims=True)
        out = (out - mean) * jax.lax.rsqrt(var + EPS)
        out = out * gn_w.reshape(H, Dh) + gn_b.reshape(H, Dh)
        out = out.reshape(B, S, D)
        gate = jax.nn.silu(x @ Wg.T)
        return gate * out @ Wo.T

    def _L1_ffn_ref(x, rw1, rb1, rw2, rb2, we1, be1, we2, be2):
        import jax, jax.numpy as jnp
        import numpy as np
        B, T, D, E, H, K = (2, 256, 128, 8, 512, 2)
        b, t, d = x.shape
        xt = x.reshape(b * t, d)
        n = xt.shape[0]
        logits = jax.nn.silu(xt @ rw1 + rb1) @ rw2 + rb2
        _, idx = jax.lax.top_k(logits, K)
        mask = jnp.zeros((n, E), bool).at[jnp.arange(n)[:, None], idx].set(True)
        w = jax.nn.softmax(jnp.where(mask, logits, -jnp.inf), axis=1)
        h = jax.nn.silu(jnp.einsum('nd,edh->enh', xt, we1) + be1[:, None, :])
        eo = jnp.einsum('enh,ehd->end', h, we2) + be2[:, None, :]
        y = xt + jnp.einsum('ne,end->nd', w, eo)
        return y.reshape(b, t, d)
    x = L0_attn_x
    x = x + 0.5 * _L0_ffn_ref(_layernorm(x, axis=-1), L0_ffn_Ws, L0_ffn_bs, L0_ffn_Wg, L0_ffn_Wu, L0_ffn_Wd)
    x = x + _L0_attn_ref(_layernorm(x, axis=-1), L0_attn_time_mix_k, L0_attn_time_mix_v, L0_attn_time_mix_r, L0_attn_time_decay, L0_attn_time_first, L0_attn_Wk, L0_attn_Wv, L0_attn_Wr, L0_attn_Wo)
    x = x + 0.5 * _L0_ffn_ref(_layernorm(x, axis=-1), L0_ffn_Ws, L0_ffn_bs, L0_ffn_Wg, L0_ffn_Wu, L0_ffn_Wd)
    x = x + 0.5 * _L1_ffn_ref(_layernorm(x, axis=-1), L1_ffn_rw1, L1_ffn_rb1, L1_ffn_rw2, L1_ffn_rb2, L1_ffn_we1, L1_ffn_be1, L1_ffn_we2, L1_ffn_be2)
    x = x + _L1_attn_ref(_layernorm(x, axis=-1), L1_attn_Wq, L1_attn_Wk, L1_attn_Wv, L1_attn_Wg, L1_attn_Wo, L1_attn_gn_w, L1_attn_gn_b)
    x = x + 0.5 * _L1_ffn_ref(_layernorm(x, axis=-1), L1_ffn_rw1, L1_ffn_rb1, L1_ffn_rw2, L1_ffn_rb2, L1_ffn_we1, L1_ffn_be1, L1_ffn_we2, L1_ffn_be2)
    return x

_drawn_inputs = setup_inputs


def setup_inputs(seed=0):
    import zlib

    import numpy as np

    out = dict(_drawn_inputs(seed))
    spreads = {'L0_ffn_bs': (0.0, 0.8),
     'L1_attn_gn_w': (1.0, 0.2),
     'L1_attn_gn_b': (0.0, 0.589),
     'L1_ffn_rb1': (0.0, 2.0),
     'L1_ffn_rb2': (0.0, 0.8),
     'L1_ffn_be1': (0.0, 0.8),
     'L1_ffn_be2': (0.0, 0.398)}
    factors = {'L0_attn_time_mix_k': 8.0,
     'L0_attn_time_mix_v': 8.0,
     'L0_attn_time_mix_r': 8.0,
     'L0_attn_time_decay': 8.0,
     'L0_attn_time_first': 8.0,
     'L0_attn_Wk': 8.0,
     'L0_attn_Wv': 3.358,
     'L0_attn_Wr': 8.0,
     'L0_attn_Wo': 3.443,
     'L0_ffn_Ws': 8.0,
     'L0_ffn_Wg': 6.939,
     'L0_ffn_Wu': 6.83,
     'L0_ffn_Wd': 6.838,
     'L1_ffn_rw1': 8.0,
     'L1_ffn_rw2': 8.0,
     'L1_ffn_we1': 4.761}
    for name, (base, spread) in spreads.items():
        noise = np.random.default_rng([zlib.crc32(name.encode()), seed]).standard_normal(out[name].shape)
        drawn = base * np.exp(spread * noise) if base else spread * noise
        out[name] = jnp.asarray(drawn.astype(out[name].dtype))
    for name, factor in factors.items():
        out[name] = (out[name] * factor).astype(out[name].dtype)
    return out
```

```python
from contextlib import ExitStack

import numpy as np

import concourse.bass as bass
from concourse import mybir

F32 = mybir.dt.float32
F32R = mybir.dt.float32r
BF16 = mybir.dt.bfloat16
I32 = mybir.dt.int32
ALU = mybir.AluOpType
ACT = mybir.ActivationFunctionType
AX = mybir.AxisListType

P = 128
NB, S = 2, 1024
T = NB * S
TG = 512
NG = T // TG
GB = S // TG
NT = TG // P
E = 8
F0, F1 = 344, 512
CH = [-(-F0 // P), -(-F1 // P)]
NCK = [E * CH[0], E * CH[1]]
W0, W1 = 2 * F0 + CH[0] * P, F1 + CH[1] * P
KIND = {0: 0, 2: 0, 3: 1, 5: 1}
CALL = {0: 0, 2: 1, 3: 0, 5: 1}
H, DH = 16, 8
NCH = S // P
EPS = 1e-5
RSQRT_MAGIC = float(0x5F3759DF)
LAG = 3
HR = 4
UPR = [2, 4]
RAW = [2, 4]
YR = 2

MIX, DECAY, FIRST, RB1, BE1 = 0, 3, 4, 5, 6
BE2 = BE1 + E * CH[1]
WS = BE2 + E
BS = WS + 2 * E
NCOL = BS + 2 * NT * E
K_AVG, K_ONES, K_ID, K_BLOCK, K_GQ, K_GK = (P * i for i in range(6))
K_TIE = 6 * P
K_QMASK = K_TIE + NT * E * E
K_G128 = K_QMASK + 4
NCONST = K_G128 + 1
M_MIX, M_O, M_QK, M_VG, M_RO, M_R1 = 0, 3 * P, 4 * P, 8 * P, 10 * P, 11 * P
NSQ = 12 * P


class Steps:

    def __init__(self, sem, names):
        self.sem, self.names = sem, list(names)

    def done(self, rnd, name):
        return rnd * len(self.names) + (self.names.index(name) + 1)


def cols(i, n):
    return bass.ds(i * n, n)


def heads(ap, *sizes):
    if len(sizes) == 2:
        return ap.rearrange("p (a b) -> p a b", a=sizes[0])
    return ap.rearrange("p (a b c) -> p a b c", a=sizes[0], b=sizes[1])


def build_block(nc, x_in, w0_in, w1_in, cols_in, sq_in, gn_in, const_in, sel_in, rope_in, decay_in, out):
    ctx = ExitStack()
    with ctx:
        def sb(name, shape, dt=F32):
            return ctx.enter_context(nc.sbuf_tensor(name, shape, dt))

        def sem(name):
            return ctx.enter_context(nc.semaphore(name))

        x = sb("x", [P, T])
        whi = sb("whi", [P, E * W0], F32R)
        wlo = sb("wlo", [P, E * W0], F32R)
        colv = sb("colv", [P, NCOL])
        sq = sb("sq", [P, NSQ])
        const = sb("const", [P, NCONST])
        sel = sb("sel", [P, E * P + P], BF16)
        gn = sb("gn", [P, 2 * P])
        xc = sb("xc", [P, TG])
        xsq = sb("xsq", [P, TG])
        stat = sb("stat", [P, 3, NT])
        diag = sb("diag", [P, TG])
        xn = sb("xn", [P, TG])
        xn_hi = sb("xn_hi", [P, T], F32R)
        xn_lo = sb("xn_lo", [P, T], F32R)
        zr = sb("zr", [P, TG])
        lg = sb("lg", [P, NT * E])
        beats = sb("beats", [P, 2, NT * E * E])
        rt = sb("rt", [P, 8, NT * E])
        cpart = sb("cpart", [P, NT, 3, E], BF16)
        cT = sb("cT", [P, T], BF16)
        raw = sb("raw", [P, 4, TG])
        h_hi = sb("h_hi", [P, HR, TG], F32R)
        h_lo = sb("h_lo", [P, HR, TG], F32R)
        cb = sb("cb", [P, YR, TG])
        ytmp = sb("ytmp", [P, TG])
        AR = 12800
        arena = sb("arena", [P, AR])
        cursor = [0]

        def carve(*shape):
            n = int(np.prod(shape))
            ap = arena[:, cursor[0]:cursor[0] + n]
            cursor[0] += n
            assert cursor[0] <= AR
            return heads(ap, *shape) if len(shape) > 1 else ap

        stage = [carve(E, W0)]
        sel_raw = carve(E * P + P)
        cursor[0] = 0
        stage.append(carve(E, W1))
        cursor[0] = 0
        SW = S + 1
        rw_xn, rw_pp, rw_aa, rw_bb = (carve(NB * SW) for _ in range(4))
        rw_ex = carve(4, TG)
        rw_th = carve(TG)
        rw_t = carve(2, TG)
        rw_w = carve(6, P)
        rw_v = carve(5)
        cursor[0] = 0
        rope = carve(2, NCH, P)
        decay = carve(H * P)
        r_t1, r_t2, r_qk, r_qkg = (carve(2 * P) for _ in range(4))
        r_v = carve(P)
        r_gate = carve(NT, P)
        r_kT, r_qgT = carve(P), carve(P)
        r_qm = carve(4, P)
        r_A = carve(H * P)
        r_kv, r_S = carve(P), carve(P)
        r_oc, r_osq, r_og, r_ogT = (carve(TG) for _ in range(4))
        r_st = carve(3, NT * H)
        r_mean = carve(NT * H)

        bank = [ctx.enter_context(nc.psum_tensor(f"bank{i}", [P, TG], F32)) for i in range(8)]
        up = bank[0:4]
        ybank = bank[4:6]
        cbank = bank[6]
        light = bank[7]
        score = [bank[3], bank[4], bank[5], bank[6]]

        ld_x = sem("ld_x")
        ld_small = sem("ld_small")
        ld_w = [sem(f"ld_w{e}") for e in range(E)]
        ld_ret = sem("ld_ret")
        st_out = sem("st_out")
        x_done = sem("x_done")
        cT_zero = sem("cT_zero")
        sel_ready = sem("sel_ready")
        split_hi = sem("split_hi")
        split_lo = sem("split_lo")

        NEWTON = [f"newton{i}{s}" for i in range(3) for s in "abc"]
        LN_PE = Steps(sem("ln_pe"), ["mean", "var", "rstd"])
        LN_ACT = Steps(sem("ln_act"), ["square"])
        LN_DVE = Steps(sem("ln_dve"), ["xc", "eps", "bits", "guess"] + NEWTON
                       + [f"diag{i}" for i in range(NT)] + ["xn"])
        ROUTE = ["lo", "lg", "gt", "eq", "tie", "beat", "rank", "sel", "lsel", "lsum", "half", "arg",
                 "half_w", "w", "p1", "r1", "p2", "r2", "p3", "cT"]
        RT_PE = [Steps(sem("rt0_pe"), ["logits", "cT"]), Steps(sem("rt1_pe"), ["z", "logits", "cT"])]
        RT_ACT = [Steps(sem("rt0_act"), ["hi", "tanh"]), Steps(sem("rt1_act"), ["hi", "z", "tanh"])]
        RT_DVE = [Steps(sem("rt0_dve"), ROUTE), Steps(sem("rt1_dve"), ["res"] + ROUTE)]

        class ExpertSems:

            def __init__(self, k):
                self.up_ready = sem(f"k{k}_up_ready")
                self.s_ready = sem(f"k{k}_s_ready")
                self.h_done = sem(f"k{k}_h_done")
                self.hi_ready = sem(f"k{k}_hi_ready")
                self.lo_ready = sem(f"k{k}_lo_ready")
                self.down_done = sem(f"k{k}_down_done")
                self.y_ready = sem(f"k{k}_y_ready")
                self.cb_ready = sem(f"k{k}_cb_ready")
                self.cb_copied = sem(f"k{k}_cb_copied")
                self.y_done = sem(f"k{k}_y_done")

        EX = [ExpertSems(0), ExpertSems(1)]

        SET_DVE = Steps(sem("set_dve"), [f"omm{i}" for i in range(3)] + [f"w{i}" for i in range(6)]
                        + ["neg", "xn0", "pp0", "aa0", "bb0"])
        SET_ACT = Steps(sem("set_act"), ["exp"])
        RW_PE = Steps(sem("rw_pe"), ["k", "v", "r", "o"])
        RW_ACT = Steps(sem("rw_act"), ["exp", "tanh"])
        RW_DVE = Steps(sem("rw_dve"), ["pp", "a1", "a2", "p", "a3", "a4", "sig", "kv", "aa", "bb", "n1", "n2",
                                       "num", "d1", "den", "rec", "wkv", "rwkv", "x"])
        RE_PE = Steps(sem("re_pe"), [s + str(c) for c in range(NT)
                                     for s in ("proj", "tr", "sc", "cross", "kv", "out")] + ["oT", "o"])
        RE_ACT = Steps(sem("re_act"), [s + str(c) for c in range(NT) for s in ("v", "gate", "kT", "qgT")]
                       + ["sq", "oT"])
        RE_DVE = Steps(sem("re_dve"), [s + str(c) for c in range(NT)
                                       for s in ("t1_", "t2_", "qk", "qg", "kg", "qm", "A0_", "A1_", "A2_", "A3_",
                                                 "kvm", "S")]
                       + ["sum", "oc", "var", "eps", "bits", "guess"] + NEWTON + ["norm", "gw", "gb", "og", "x"])
        RE_ZERO = sem("re_zero")

        block = ctx.enter_context(nc.Block())

        def rows(k, c):
            return min(P, (F0, F1)[k] - c * P)

        def up_w(w, k, e, c):
            n = rows(k, c)
            starts = [e * W0 + c * P, e * W0 + F0 + c * P] if k == 0 else [e * W1 + c * P]
            return [w[:, s:s + n] for s in starts]

        def down_w(w, k, e, c):
            s = e * W0 + 2 * F0 + c * P if k == 0 else e * W1 + F1 + c * P
            return w[0:rows(k, c), s:s + P]

        def slots(k, c):
            return (c % 2, 2 + c % 2) if k == 0 else (c % 4, c % 4)

        def row_part(buf, b, half, shift):
            return buf[:, bass.ds(b * SW + (half * TG + shift), TG)]

        def units(eng, run):
            with eng.Fori(0, NG - 1) as g:
                run(g, True)
            run(NG - 1, False)

        @block.sync
        def _(sp):
            sp.dma_start(x[:], x_in).then_inc(ld_x, 16)
            for dst, src in ((const, const_in), (colv, cols_in), (sel_raw, sel_in), (sq, sq_in), (gn, gn_in)):
                sp.dma_start(dst[:, :], src).then_inc(ld_small, 16)
            for e in range(E):
                sp.dma_start(stage[0][:, e, :], w0_in[e, :, :]).then_inc(ld_w[e], 16)
            sp.wait_ge(x_done, 2 * NG)
            for e in range(E):
                sp.dma_start(stage[1][:, e, :], w1_in[e, :, :]).then_inc(ld_w[e], 16)
            sp.wait_ge(split_hi, 2 * E)
            sp.wait_ge(split_lo, 2 * E)
            sp.dma_start(rope, rope_in).then_inc(ld_ret, 16)
            sp.dma_start(decay, decay_in).then_inc(ld_ret, 16)
            for g in range(NG):
                sp.wait_ge(x_done, 5 * NG + g + 1)
                sp.dma_start(out[:, g * TG:(g + 1) * TG], x[:, g * TG:(g + 1) * TG]).then_inc(st_out, 16)
            sp.wait_ge(st_out, 16 * NG)

        @block.tensor
        def _(pe):
            mm = nc.tensor.matmul

            def after(steps, rnd, name):
                pe.wait_ge(steps.sem, steps.done(rnd, name))

            def ln_mean(f, g):
                mm(light[:], const[:, K_AVG:K_AVG + P], x[:, cols(g, TG)], start=True, stop=True)\
                    .then_inc(LN_PE.sem, 1)

            def ln_var(f, g):
                after(LN_ACT, f * NG + g, "square")
                for i in range(NT):
                    last = mm(light[:, i:i + 1], xsq[:, i * P:(i + 1) * P], const[:, K_AVG:K_AVG + 1],
                              start=True, stop=True)
                last.then_inc(LN_PE.sem, 1)

            def ln_rstd(f, g):
                after(LN_DVE, f * NG + g, f"diag{NT - 1}")
                mm(light[:], const[:, K_ONES:K_ONES + P], diag[:], start=True, stop=True).then_inc(LN_PE.sem, 1)

            def prep(f, g, s):
                k = KIND[f]
                v = CALL[f] * NG + g
                if s == 0:
                    if f > 0:
                        pe.wait_ge(x_done, (f - 1) * NG + g + 1)
                    ln_mean(f, g)
                elif s == 1:
                    ln_var(f, g)
                elif s == 2:
                    ln_rstd(f, g)
                elif s == 3 and k == 1:
                    after(LN_DVE, f * NG + g, "xn")
                    mm(light[:], sq[:, M_R1:M_R1 + P], xn[:], start=True, stop=True).then_inc(RT_PE[1].sem, 1)
                elif s == 4:
                    if k == 0:
                        after(LN_DVE, f * NG + g, "xn")
                    else:
                        after(RT_ACT[1], v, "z")
                    src = (xn, zr)[k]
                    for i in range(NT):
                        last = mm(light[:, i * E:(i + 1) * E], src[:, i * P:(i + 1) * P],
                                  colv[:, WS + k * E:WS + (k + 1) * E], start=True, stop=True)
                    last.then_inc(RT_PE[k].sem, 1)
                elif s == 6:
                    after(RT_DVE[k], v, "p3")
                    for i in range(NT):
                        last = nc.tensor.transpose(light[:].bitcast(BF16)[0:3 * E, i * P:(i + 1) * P],
                                                   cpart[:, i, :, :].rearrange("p a b -> p (a b)"),
                                                   sel[:, E * P:E * P + P])
                    last.then_inc(RT_PE[k].sem, 1)

            def unit(f, g, prep_next):
                k = KIND[f]
                ex, ch, nck = EX[k], CH[k], NCK[k]
                v = CALL[f] * NG + g
                nup = 2 if k == 0 else 1
                xhi, xlo = xn_hi[:, cols(g, TG)], xn_lo[:, cols(g, TG)]
                after(RT_DVE[k], v, "lo")
                for step in range(nck + LAG):
                    if step < nck:
                        e, c = divmod(step, ch)
                        if c == 0:
                            pe.wait_ge(ex.cb_copied, v * E + (e + 1))
                            if e == 0:
                                after(RT_DVE[k], v, "cT")
                            mm(cbank[:], sel[:, e * P:(e + 1) * P], cT[:, cols(g, TG)],
                               start=True, stop=True).then_inc(ex.cb_ready, 1)
                            pe.wait_ge(split_lo, k * E + e + 1)
                        pe.wait_ge(ex.h_done if k == 0 else ex.s_ready, v * nck + (step + 1))
                        for j in range(nup):
                            po = up[(step % UPR[k]) * nup + j][0:rows(k, c), :]
                            hi, lo = up_w(whi, k, e, c)[j], up_w(wlo, k, e, c)[j]
                            mm(po, hi, xhi, start=True, stop=False)
                            mm(po, hi, xlo, start=False, stop=False)
                            last = mm(po, lo, xhi, start=False, stop=True)
                        last.then_inc(ex.up_ready, 1)
                        if prep_next and c == 2:
                            prep(f, g + 1, e)
                    if step >= LAG:
                        i = step - LAG
                        e, c = divmod(i, ch)
                        if c == 0:
                            pe.wait_ge(ex.y_done, 2 * v * E + (2 * e + 1))
                        pe.wait_ge(ex.hi_ready, v * nck + (i + 1))
                        pe.wait_ge(ex.lo_ready, v * nck + (i + 1 + RAW[k]))
                        n, po = rows(k, c), ybank[e % YR][:]
                        hi, lo = down_w(whi, k, e, c), down_w(wlo, k, e, c)
                        mm(po, hi, h_hi[0:n, i % HR, :], start=(c == 0), stop=False)
                        mm(po, lo, h_hi[0:n, i % HR, :], start=False, stop=False)
                        mm(po, hi, h_lo[0:n, i % HR, :], start=False, stop=(c == ch - 1)).then_inc(ex.down_done, 1)

            def experts(f):
                pe.wait_ge(x_done, f * NG) if f else pe.wait_ge(ld_x, 16)
                for s in range(E):
                    prep(f, 0, s)
                units(pe, lambda g, more: unit(f, g, more))

            def rwkv(b, half):
                g = b * GB + half
                r = g
                pe.wait_ge(x_done, NG + g)
                ln_mean(1, g)
                ln_var(1, g)
                ln_rstd(1, g)
                after(LN_DVE, NG + g, "xn")
                for j in range(3):
                    mm(up[j][:], rw_w[:, 2 * j, :], row_part(rw_xn, b, half, 1), start=True, stop=False)
                    mm(up[j][:], rw_w[:, 2 * j + 1, :], row_part(rw_xn, b, half, 0), start=False, stop=True)\
                        .then_inc(RW_PE.sem, 1)
                after(RW_DVE, r, "rwkv")
                mm(light[:], sq[:, M_O:M_O + P], rw_t[:, 0, :], start=True, stop=True).then_inc(RW_PE.sem, 1)

            def retention(b, half):
                g = b * GB + half
                pe.wait_ge(x_done, 4 * NG + g)
                ln_mean(4, g)
                ln_var(4, g)
                ln_rstd(4, g)
                after(LN_DVE, 4 * NG + g, "xn")
                ident = const[:, K_ID:K_ID + P]
                for c in range(NT):
                    xt = xn[:, c * P:(c + 1) * P]
                    if c:
                        after(RE_DVE, g, f"t2_{c - 1}")
                        after(RE_ACT, g, f"gate{c - 1}")
                    mm(up[0][:], xt, sq[:, M_QK:M_QK + 4 * P], start=True, stop=True)
                    mm(up[1][:, 0:2 * P], xt, sq[:, M_VG:M_VG + 2 * P], start=True, stop=True).then_inc(RE_PE.sem, 1)
                    if c:
                        after(RE_DVE, g, f"S{c - 1}")
                    after(RE_DVE, g, f"kg{c}")
                    for j, src in enumerate((r_qk[:, 0:P], r_qk[:, P:2 * P], r_qkg[:, 0:P])):
                        last = nc.tensor.transpose(up[2][:, j * P:(j + 1) * P], src, ident)
                    last.then_inc(RE_PE.sem, 1)
                    after(RE_ACT, g, f"qgT{c}")
                    after(RE_DVE, g, f"qm{c}")
                    for q in range(4):
                        rs = slice(32 * q, 32 * q + 32)
                        last = mm(score[q][:], r_kT[rs, :], r_qm[rs, :, :].rearrange("p a b -> p (a b)"),
                                  start=True, stop=True)
                    last.then_inc(RE_PE.sem, 1)
                    if c == 0 and half == 0:
                        pe.wait_ge(RE_ZERO, b + 1)
                    elif c == 0:
                        after(RE_DVE, g - 1, f"S{NT - 1}")
                    o = light[:, c * P:(c + 1) * P]
                    mm(o, r_qgT, r_S, start=True, stop=False, skip_group_check=True).then_inc(RE_PE.sem, 1)
                    after(RE_ACT, g, f"v{c}")
                    mm(up[2][:, 3 * P:4 * P], r_qkg[:, P:2 * P], r_v, start=True, stop=True).then_inc(RE_PE.sem, 1)
                    after(RE_DVE, g, f"A3_{c}")
                    for h in range(H):
                        last = mm(o[:, h * DH:(h + 1) * DH], r_A[:, h * P:(h + 1) * P], r_v[:, h * DH:(h + 1) * DH],
                                  start=False, stop=(h == H - 1), skip_group_check=True)
                    last.then_inc(RE_PE.sem, 1)
                after(RE_DVE, g, "og")
                for c in range(NT):
                    last = nc.tensor.transpose(up[2][:, c * P:(c + 1) * P], r_og[:, c * P:(c + 1) * P], ident)
                last.then_inc(RE_PE.sem, 1)
                after(RE_ACT, g, "oT")
                mm(light[:], sq[:, M_RO:M_RO + P], r_ogT, start=True, stop=True).then_inc(RE_PE.sem, 1)

            def rows_of_batch(run):
                with pe.Fori(0, NB) as b:
                    for half in range(GB):
                        run(b, half)

            for k in range(2):
                pe.sem_inc(EX[k].down_done, HR)
            pe.wait_ge(ld_small, 16 * 5)
            pe.wait_ge(cT_zero, 1)
            pe.wait_ge(sel_ready, 1)
            experts(0)
            after(SET_DVE, 0, "bb0")
            rows_of_batch(rwkv)
            experts(2)
            experts(3)
            rows_of_batch(retention)
            experts(5)

        @block.scalar
        def _(act):
            def after(steps, rnd, name):
                act.wait_ge(steps.sem, steps.done(rnd, name))

            def split_weights(k):
                w = (W0, W1)[k]
                if k:
                    act.wait_ge(EX[0].down_done, 2 * NG * NCK[0] + HR)
                for e in range(E):
                    act.wait_ge(ld_w[e], 16 * (k + 1))
                    nc.scalar.activation(whi[:, e * w:(e + 1) * w], stage[k][:, e, :], ACT.Copy).then_inc(split_hi, 1)

            def ln_square(f, g):
                after(LN_DVE, f * NG + g, "xc")
                nc.scalar.activation(xsq[:], xc[:], ACT.Square).then_inc(LN_ACT.sem, 1)

            def prep(f, g, s):
                k = KIND[f]
                v = CALL[f] * NG + g
                if s == 0:
                    ln_square(f, g)
                elif s == 2:
                    after(LN_DVE, f * NG + g, "xn")
                    nc.scalar.activation(xn_hi[:, cols(g, TG)], xn[:], ACT.Copy).then_inc(RT_ACT[k].sem, 1)
                elif s == 3 and k == 1:
                    after(RT_PE[1], v, "z")
                    nc.scalar.activation(zr[:], light[:], ACT.Silu, bias=colv[:, RB1:RB1 + 1]).then_inc(RT_ACT[1].sem, 1)
                elif s == 4:
                    after(RT_DVE[k], v, "arg")
                    nc.scalar.activation(rt[:, 5, :], rt[:, 4, :], ACT.Tanh).then_inc(RT_ACT[k].sem, 1)

            def unit(f, g, prep_next):
                k = KIND[f]
                ex, ch, nck = EX[k], CH[k], NCK[k]
                v = CALL[f] * NG + g
                for step in range(nck + 1):
                    if step < nck:
                        e, c = divmod(step, ch)
                        n = rows(k, c)
                        if c == 0:
                            act.wait_ge(ex.y_done, 2 * v * E + (2 * e + 1))
                            act.wait_ge(ex.cb_ready, v * E + (e + 1))
                            nc.scalar.activation(cb[:, e % YR, :], cbank[:], ACT.Copy).then_inc(ex.cb_copied, 1)
                        act.wait_ge(ex.up_ready, v * nck + (step + 1))
                        act.wait_ge(ex.h_done if k == 0 else ex.lo_ready, v * nck + (step + 1))
                        src = up[(step % UPR[k]) * (2 if k == 0 else 1)][0:n, :]
                        dst = raw[0:n, slots(k, step)[0], :]
                        if k == 0:
                            nc.scalar.activation(dst, src, ACT.Silu).then_inc(ex.s_ready, 1)
                        else:
                            j = BE1 + e * ch + c
                            nc.scalar.activation(dst, src, ACT.Silu, bias=colv[:, j:j + 1]).then_inc(ex.s_ready, 1)
                        if prep_next and c == 1 and e:
                            prep(f, g + 1, e - 1)
                    if step and k == 0:
                        i = step - 1
                        n = rows(k, i % ch)
                        act.wait_ge(ex.h_done, v * nck + (i + 1 + RAW[0]))
                        act.wait_ge(ex.down_done, v * nck + (i + 1))
                        nc.scalar.activation(h_hi[0:n, i % HR, :], raw[0:n, slots(k, i)[1], :], ACT.Copy)\
                            .then_inc(ex.hi_ready, 1)
                if prep_next:
                    prep(f, g + 1, E - 1)

            def experts(f):
                for s in range(E):
                    prep(f, 0, s)
                units(act, lambda g, more: unit(f, g, more))

            def rwkv(b, half):
                g = b * GB + half
                ln_square(1, g)
                after(RW_DVE, g, "a4")
                ex = rw_ex.rearrange("p a b -> p (a b)")
                nc.scalar.activation(ex, ex, ACT.Exp).then_inc(RW_ACT.sem, 1)
                after(RW_PE, g, "r")
                nc.scalar.activation(rw_th, up[2][:], ACT.Tanh, scale=0.5).then_inc(RW_ACT.sem, 1)

            def retention(b, half):
                g = b * GB + half
                ln_square(4, g)
                for c in range(NT):
                    after(RE_PE, g, f"proj{c}")
                    if c:
                        after(RE_PE, g, f"out{c - 1}")
                    nc.scalar.activation(r_v, up[1][:, 0:P], ACT.Copy).then_inc(RE_ACT.sem, 1)
                    nc.scalar.activation(r_gate[:, c, :], up[1][:, P:2 * P], ACT.Silu).then_inc(RE_ACT.sem, 1)
                    after(RE_PE, g, f"tr{c}")
                    nc.scalar.activation(r_kT, up[2][:, P:2 * P], ACT.Copy).then_inc(RE_ACT.sem, 1)
                    nc.scalar.activation(r_qgT, up[2][:, 2 * P:3 * P], ACT.Copy).then_inc(RE_ACT.sem, 1)
                after(RE_DVE, g, "oc")
                nc.scalar.activation(r_osq, r_oc, ACT.Square).then_inc(RE_ACT.sem, 1)
                after(RE_PE, g, "oT")
                nc.scalar.activation(r_ogT, up[2][:], ACT.Copy).then_inc(RE_ACT.sem, 1)

            def rows_of_batch(run):
                with act.Fori(0, NB) as b:
                    for half in range(GB):
                        run(b, half)

            act.sem_inc(EX[1].s_ready, UPR[1])
            for k in range(2):
                act.sem_inc(EX[k].cb_copied, 1)
            act.wait_ge(ld_small, 16 * 5)
            split_weights(0)
            experts(0)
            after(SET_DVE, 0, "omm2")
            nc.scalar.activation(rw_v[:, 3:4], colv[:, DECAY:DECAY + 1], ACT.Exp).then_inc(SET_ACT.sem, 1)
            rows_of_batch(rwkv)
            experts(2)
            split_weights(1)
            experts(3)
            act.wait_ge(ld_ret, 32)
            rows_of_batch(retention)
            experts(5)

        @block.gpsimd
        def _(pool):
            for k in range(2):
                pool.sem_inc(EX[k].lo_ready, RAW[k])

            def unit(f, g, prep_next):
                k = KIND[f]
                ex, ch, nck = EX[k], CH[k], NCK[k]
                v = CALL[f] * NG + g
                for i in range(nck):
                    n = rows(k, i % ch)
                    pool.wait_ge(ex.hi_ready, v * nck + (i + 1))
                    pool.wait_ge(ex.down_done, v * nck + (i + 1))
                    nc.gpsimd.tensor_tensor(h_lo[0:n, i % HR, :], raw[0:n, slots(k, i)[1], :],
                                            h_hi[0:n, i % HR, :].bitcast(F32), ALU.subtract).then_inc(ex.lo_ready, 1)

            for f in (0, 2, 3, 5):
                units(pool, lambda g, more, f=f: unit(f, g, more))

        @block.vector
        def _(dve):
            V = nc.vector

            def after(steps, rnd, name):
                dve.wait_ge(steps.sem, steps.done(rnd, name))

            def split_weights(k):
                w = (W0, W1)[k]
                for e in range(E):
                    dve.wait_ge(split_hi, k * E + e + 1)
                    c = slice(e * w, (e + 1) * w)
                    V.tensor_tensor(wlo[:, c], stage[k][:, e, :], whi[:, c].bitcast(F32), ALU.subtract)\
                        .then_inc(split_lo, 1)

            def rsqrt(steps, r, var, y, t):
                after(steps, r, "eps")
                V.tensor_scalar(t.bitcast(I32), var.bitcast(I32), 1, None, ALU.logical_shift_right).then_inc(steps.sem, 1)
                after(steps, r, "bits")
                V.tensor_scalar(y.bitcast(I32), t.bitcast(I32), -1.0, RSQRT_MAGIC, ALU.mult, ALU.add)\
                    .then_inc(steps.sem, 1)
                last = "guess"
                for i in range(3):
                    after(steps, r, last)
                    V.scalar_tensor_tensor(t, y, -0.5, y, ALU.mult, ALU.mult).then_inc(steps.sem, 1)
                    after(steps, r, f"newton{i}a")
                    V.tensor_tensor(t, t, var, ALU.mult).then_inc(steps.sem, 1)
                    after(steps, r, f"newton{i}b")
                    V.scalar_tensor_tensor(y, t, 1.5, y, ALU.add, ALU.mult).then_inc(steps.sem, 1)
                    last = f"newton{i}c"
                after(steps, r, last)

            def ln_center(f, g):
                after(LN_PE, f * NG + g, "mean")
                V.tensor_tensor(xc[:], x[:, cols(g, TG)], light[:], ALU.subtract).then_inc(LN_DVE.sem, 1)

            def ln_rstd(f, g):
                n = f * NG + g
                after(LN_PE, n, "var")
                V.tensor_scalar(stat[:, 0, :], light[:, 0:NT], EPS, None, ALU.add).then_inc(LN_DVE.sem, 1)
                rsqrt(LN_DVE, n, stat[:, 0, :], stat[:, 1, :], stat[:, 2, :])
                for i in range(NT):
                    V.tensor_scalar(diag[:, i * P:(i + 1) * P], const[:, K_ID:K_ID + P], stat[:, 1, i:i + 1], None,
                                    ALU.mult).then_inc(LN_DVE.sem, 1)

            def ln_scale(f, g, dst):
                after(LN_PE, f * NG + g, "rstd")
                V.tensor_tensor(dst, xc[:], light[:], ALU.mult).then_inc(LN_DVE.sem, 1)

            def prep(f, g, s):
                k = KIND[f]
                v = CALL[f] * NG + g
                R = RT_DVE[k]

                def step(ins):
                    ins.then_inc(R.sem, 1)

                def view(i):
                    return heads(rt[:, i, :], NT, E)

                if s == 0:
                    ln_center(f, g)
                elif s == 1:
                    ln_rstd(f, g)
                elif s == 2:
                    ln_scale(f, g, xn[:])
                elif s == 3:
                    xg = x[:, cols(g, TG)]
                    if k == 1:
                        after(LN_DVE, f * NG + g, "xn")
                        step(V.scalar_tensor_tensor(xg, xn[:], 0.5, xg, ALU.mult, ALU.add))
                    after(RT_ACT[k], v, "hi")
                    step(V.tensor_tensor(xn_lo[:, cols(g, TG)], xn[:], xn_hi[:, cols(g, TG)].bitcast(F32),
                                         ALU.subtract))
                elif s == 4:
                    after(RT_PE[k], v, "logits")
                    b = BS + k * NT * E
                    step(V.tensor_tensor(lg[:], light[:, 0:NT * E], colv[:, b:b + NT * E], ALU.add))
                    after(R, v, "lg")
                    one = heads(lg[:], NT, E).unsqueeze(3).to_broadcast([P, NT, E, E])
                    other = heads(lg[:], NT, E).unsqueeze(2).to_broadcast([P, NT, E, E])
                    gt, eq = beats[:, 0, :], beats[:, 1, :]
                    step(V.tensor_tensor(heads(gt, NT, E, E), other, one, ALU.is_gt))
                    step(V.tensor_tensor(heads(eq, NT, E, E), other, one, ALU.is_equal))
                    after(R, v, "eq")
                    step(V.tensor_tensor(eq, eq, const[:, K_TIE:K_TIE + NT * E * E], ALU.mult))
                    after(R, v, "tie")
                    step(V.tensor_tensor(gt, gt, eq, ALU.add))
                    after(R, v, "beat")
                    step(V.tensor_reduce(rt[:, 0, :], gt.rearrange("p (a b) -> p a b", b=E), AX.X, ALU.add))
                    after(R, v, "rank")
                    step(V.tensor_scalar(rt[:, 1, :], rt[:, 0, :], 1.5, None, ALU.is_lt))
                    after(R, v, "sel")
                    step(V.tensor_tensor(rt[:, 2, :], lg[:], rt[:, 1, :], ALU.mult))
                    after(R, v, "lsel")
                    step(V.tensor_reduce(rt[:, 3, 0:NT], view(2), AX.X, ALU.add))
                    after(R, v, "lsum")
                    step(V.tensor_scalar(rt[:, 3, NT:2 * NT], rt[:, 3, 0:NT], -0.5, None, ALU.mult))
                    after(R, v, "half")
                    step(V.tensor_tensor(view(4), heads(lg[:], NT, E),
                                         rt[:, 3, NT:2 * NT].unsqueeze(2).to_broadcast([P, NT, E]), ALU.add))
                elif s == 5:
                    after(RT_ACT[k], v, "tanh")
                    step(V.tensor_scalar(rt[:, 6, :], rt[:, 5, :], 0.25, 0.25, ALU.mult, ALU.add))
                    after(R, v, "half_w")
                    step(V.tensor_tensor(rt[:, 7, :], rt[:, 6, :], rt[:, 1, :], ALU.mult))
                    after(R, v, "w")
                    step(V.tensor_copy(cpart[:, :, 0, :], view(7)))
                    after(R, v, "p1")
                    step(V.tensor_tensor(view(2), view(7), cpart[:, :, 0, :], ALU.subtract))
                    after(R, v, "r1")
                    step(V.tensor_copy(cpart[:, :, 1, :], view(2)))
                    after(R, v, "p2")
                    step(V.tensor_tensor(view(6), view(2), cpart[:, :, 1, :], ALU.subtract))
                    after(R, v, "r2")
                    step(V.tensor_copy(cpart[:, :, 2, :], view(6)))
                elif s == 6:
                    after(RT_PE[k], v, "cT")
                    step(V.tensor_copy(cT[0:3 * E, cols(g, TG)], light[:].bitcast(BF16)[0:3 * E, 0:TG]))

            def unit(f, g, prep_next):
                k = KIND[f]
                ex, ch, nck = EX[k], CH[k], NCK[k]
                v = CALL[f] * NG + g
                xg = x[:, cols(g, TG)]
                for step in range(nck + LAG):
                    if step < nck:
                        e, c = divmod(step, ch)
                        n = rows(k, c)
                        s_slot, h_slot = slots(k, step)
                        if k == 0:
                            dve.wait_ge(ex.s_ready, v * nck + (step + 1))
                            dve.wait_ge(ex.lo_ready, v * nck + (step + 1))
                            V.tensor_tensor(raw[0:n, h_slot, :], raw[0:n, s_slot, :],
                                            up[(step % UPR[k]) * 2 + 1][0:n, :], ALU.mult).then_inc(ex.h_done, 1)
                        else:
                            dve.wait_ge(ex.s_ready, v * nck + (step + 1 + UPR[1]))
                            dve.wait_ge(ex.down_done, v * nck + (step + 1))
                            V.tensor_copy(h_hi[0:n, step % HR, :], raw[0:n, h_slot, :]).then_inc(ex.hi_ready, 1)
                    if step >= LAG and (step - LAG) % ch == ch - 1:
                        e = (step - LAG) // ch
                        yd = 2 * v * E + (2 * e + 2 * YR)
                        dve.wait_ge(ex.down_done, v * nck + (step - LAG + 1 + HR))
                        dve.wait_ge(ex.cb_copied, v * E + (e + 2))
                        dve.wait_ge(ex.y_done, yd)
                        yb, w = ybank[e % YR][:], cb[:, e % YR, :]
                        if k == 0:
                            V.tensor_tensor(ytmp[:], yb, w, ALU.mult).then_inc(ex.y_done, 1)
                        else:
                            V.scalar_tensor_tensor(ytmp[:], yb, colv[:, BE2 + e:BE2 + e + 1], w, ALU.add, ALU.mult)\
                                .then_inc(ex.y_done, 1)
                        dve.wait_ge(ex.y_done, yd + 1)
                        V.tensor_tensor(xg, xg, ytmp[:], ALU.add).then_inc(ex.y_done, 1)
                    if step < nck and prep_next and step % ch == ch - 1:
                        prep(f, g + 1, step // ch)
                dve.wait_ge(ex.y_done, 2 * (v + 1) * E + 2 * YR)
                dve.sem_inc(x_done, 1)

            def experts(f):
                for s in range(E):
                    prep(f, 0, s)
                units(dve, lambda g, more: unit(f, g, more))

            def rwkv_setup():
                def step(ins):
                    ins.then_inc(SET_DVE.sem, 1)

                for j in range(3):
                    step(V.tensor_scalar(rw_v[:, j:j + 1], colv[:, MIX + j:MIX + j + 1], -1.0, 1.0, ALU.mult, ALU.add))
                after(SET_DVE, 0, "omm2")
                for j in range(3):
                    w = sq[:, M_MIX + j * P:M_MIX + (j + 1) * P]
                    step(V.tensor_scalar(rw_w[:, 2 * j, :], w, colv[:, MIX + j:MIX + j + 1], None, ALU.mult))
                    step(V.tensor_scalar(rw_w[:, 2 * j + 1, :], w, rw_v[:, j:j + 1], None, ALU.mult))
                after(SET_ACT, 0, "exp")
                step(V.tensor_scalar(rw_v[:, 4:5], rw_v[:, 3:4], -1.0, None, ALU.mult))
                for buf, value in ((rw_xn, 0.0), (rw_pp, -1e30), (rw_aa, 0.0), (rw_bb, 0.0)):
                    step(V.memset(buf.rearrange("p (b s) -> p b s", b=NB)[:, :, 0:1], value))
                after(SET_DVE, 0, "bb0")

            def rwkv(b, half):
                g = b * GB + half
                r = g
                ln_center(1, g)
                ln_rstd(1, g)
                ln_scale(1, g, row_part(rw_xn, b, half, 1))

                def step(ins):
                    ins.then_inc(RW_DVE.sem, 1)

                k, v = up[0][:], up[1][:]
                w, u = rw_v[:, 4:5], colv[:, FIRST:FIRST + 1]
                pp0, pp1, aa0, aa1, bb0, bb1 = (row_part(buf, b, half, s) for buf in (rw_pp, rw_aa, rw_bb)
                                                for s in (0, 1))

                def before(buf):
                    return buf[:, bass.ds(b * SW + half * TG, 1)]

                e1b, e2b, e1, e2 = (rw_ex[:, i, :] for i in range(4))
                t0, t1 = rw_t[:, 0, :], rw_t[:, 1, :]
                after(RW_PE, r, "k")
                step(V.tensor_tensor_scan(pp1, w.to_broadcast([P, TG]), k, before(rw_pp), ALU.add, ALU.max))
                after(RW_DVE, r, "pp")
                step(V.scalar_tensor_tensor(e1b, pp0, w, pp1, ALU.add, ALU.subtract))
                step(V.tensor_tensor(e2b, k, pp1, ALU.subtract))
                step(V.scalar_tensor_tensor(t0, k, u, pp0, ALU.add, ALU.max))
                after(RW_DVE, r, "p")
                step(V.tensor_tensor(e1, pp0, t0, ALU.subtract))
                step(V.scalar_tensor_tensor(e2, k, u, t0, ALU.add, ALU.subtract))
                after(RW_ACT, r, "tanh")
                step(V.tensor_scalar(rw_th, rw_th, 0.5, 0.5, ALU.mult, ALU.add))
                after(RW_PE, r, "v")
                step(V.tensor_tensor(t1, e2b, v, ALU.mult))
                after(RW_DVE, r, "kv")
                step(V.tensor_tensor_scan(aa1, e1b, t1, before(rw_aa), ALU.mult, ALU.add))
                step(V.tensor_tensor_scan(bb1, e1b, e2b, before(rw_bb), ALU.mult, ALU.add))
                after(RW_DVE, r, "bb")
                step(V.tensor_tensor(t0, e1, aa0, ALU.mult))
                step(V.tensor_tensor(t1, e2, v, ALU.mult))
                after(RW_DVE, r, "n2")
                step(V.tensor_tensor(t0, t0, t1, ALU.add))
                after(RW_DVE, r, "num")
                step(V.tensor_tensor(t1, e1, bb0, ALU.mult))
                after(RW_DVE, r, "d1")
                step(V.tensor_tensor(t1, t1, e2, ALU.add))
                after(RW_DVE, r, "den")
                step(V.reciprocal(e1, t1))
                after(RW_DVE, r, "rec")
                step(V.tensor_tensor(t0, t0, e1, ALU.mult))
                after(RW_DVE, r, "wkv")
                step(V.tensor_tensor(t0, t0, rw_th, ALU.mult))
                after(RW_PE, r, "o")
                xg = x[:, cols(g, TG)]
                step(V.tensor_tensor(xg, xg, light[:], ALU.add))
                after(RW_DVE, r, "x")
                dve.sem_inc(x_done, 1)

            def retention(b, half):
                g = b * GB + half
                ln_center(4, g)
                ln_rstd(4, g)
                ln_scale(4, g, xn[:])
                if half == 0:
                    V.memset(r_S, 0.0).then_inc(RE_ZERO, 1)

                def step(ins):
                    ins.then_inc(RE_DVE.sem, 1)

                for c in range(NT):
                    j = half * NT + c
                    after(RE_PE, g, f"proj{c}")
                    for i, dst in enumerate((r_t1, r_t2)):
                        table = rope[:, i, j, :].unsqueeze(1).to_broadcast([P, 2, P])
                        step(V.tensor_tensor(heads(dst, 2, P), heads(up[0][:, i * 2 * P:(i + 1) * 2 * P], 2, P), table,
                                             ALU.mult))
                    after(RE_DVE, g, f"t2_{c}")
                    step(V.tensor_tensor(r_qk, r_t1, r_t2, ALU.add))
                    after(RE_DVE, g, f"qk{c}")
                    step(V.tensor_tensor(r_qkg[:, 0:P], r_qk[:, 0:P], const[:, K_GQ:K_GQ + P], ALU.mult))
                    step(V.tensor_tensor(r_qkg[:, P:2 * P], r_qk[:, P:2 * P], const[:, K_GK:K_GK + P], ALU.mult))
                    after(RE_ACT, g, f"qgT{c}")
                    step(V.tensor_tensor(r_qm, up[2][:, 0:P].unsqueeze(1).to_broadcast([P, 4, P]),
                                         const[:, K_QMASK:K_QMASK + 4].unsqueeze(2).to_broadcast([P, 4, P]), ALU.mult))
                    after(RE_PE, g, f"sc{c}")
                    for q in range(4):
                        step(V.tensor_tensor(r_A[:, q * TG:(q + 1) * TG], score[q][:], decay[:, q * TG:(q + 1) * TG],
                                             ALU.mult))
                    after(RE_PE, g, f"kv{c}")
                    step(V.tensor_tensor(r_kv, up[2][:, 3 * P:4 * P], const[:, K_BLOCK:K_BLOCK + P], ALU.mult))
                    after(RE_DVE, g, f"kvm{c}")
                    if half == 0 and c == 0:
                        dve.wait_ge(RE_ZERO, b + 1)
                    step(V.scalar_tensor_tensor(r_S, r_S, const[:, K_G128:K_G128 + 1], r_kv, ALU.mult, ALU.add))
                after(RE_PE, g, f"out{NT - 1}")
                o, oc = heads(light[:], NT * H, DH), heads(r_oc, NT * H, DH)

                def per_head(ap):
                    return ap.unsqueeze(2).to_broadcast([P, NT * H, DH])

                var, y, t = (r_st[:, i, :] for i in range(3))
                step(V.tensor_reduce(r_mean, o, AX.X, ALU.add))
                after(RE_DVE, g, "sum")
                step(V.scalar_tensor_tensor(oc, per_head(r_mean), -1.0 / DH, o, ALU.mult, ALU.add))
                after(RE_ACT, g, "sq")
                step(V.tensor_reduce(var, heads(r_osq, NT * H, DH), AX.X, ALU.add))
                after(RE_DVE, g, "var")
                step(V.tensor_scalar(var, var, 1.0 / DH, EPS, ALU.mult, ALU.add))
                rsqrt(RE_DVE, g, var, y, t)
                step(V.tensor_tensor(heads(r_og, NT * H, DH), oc, per_head(y), ALU.mult))
                last = "norm"
                for i, (name, op) in enumerate((("gw", ALU.mult), ("gb", ALU.add))):
                    after(RE_DVE, g, last)
                    par = gn[:, i * P:(i + 1) * P].unsqueeze(1).to_broadcast([P, NT, P])
                    step(V.tensor_tensor(heads(r_og, NT, P), heads(r_og, NT, P), par, op))
                    last = name
                after(RE_DVE, g, last)
                step(V.tensor_tensor(heads(r_og, NT, P), heads(r_og, NT, P), r_gate, ALU.mult))
                after(RE_PE, g, "o")
                xg = x[:, cols(g, TG)]
                step(V.tensor_tensor(xg, xg, light[:], ALU.add))
                after(RE_DVE, g, "x")
                dve.sem_inc(x_done, 1)

            def rows_of_batch(run):
                with dve.Fori(0, NB) as b:
                    for half in range(GB):
                        run(b, half)

            V.memset(cT[:], 0.0).then_inc(cT_zero, 1)
            dve.sem_inc(EX[0].h_done, UPR[0])
            for k in range(2):
                dve.sem_inc(EX[k].y_done, 2 * YR)
            dve.wait_ge(ld_small, 16 * 5)
            V.tensor_copy(sel[:], sel_raw).then_inc(sel_ready, 1)
            dve.wait_ge(cT_zero, 1)
            split_weights(0)
            experts(0)
            rwkv_setup()
            rows_of_batch(rwkv)
            experts(2)
            split_weights(1)
            experts(3)
            rows_of_batch(retention)
            experts(5)


def constants():
    f32 = np.float32
    p = np.arange(P)
    gamma = 1.0 - 2.0 ** (-5.0 - np.arange(H, dtype=np.float64))
    const = np.zeros((P, NCONST), f32)
    const[:, K_AVG:K_AVG + P] = 1.0 / P
    const[:, K_ONES:K_ONES + P] = 1.0
    const[:, K_ID:K_ID + P] = np.eye(P)
    const[:, K_BLOCK:K_BLOCK + P] = p[:, None] // DH == p[None, :] // DH
    head = gamma[p // DH]
    const[:, K_GQ:K_GQ + P] = DH ** -0.5 * head[None, :] ** (p[:, None] + 1.0)
    const[:, K_GK:K_GK + P] = head[None, :] ** (P - 1.0 - p[:, None])
    tie = np.arange(E)[None, :] < np.arange(E)[:, None]
    const[:, K_TIE:K_TIE + NT * E * E] = np.tile(tie.ravel(), NT)[None, :]
    const[:, K_QMASK:K_QMASK + 4] = (p[:, None] % 32) // DH == np.arange(4)[None, :]
    const[:, K_G128] = head ** float(P)
    diff = p[None, :] - p[:, None]
    decay = np.where(diff >= 0, gamma[:, None, None] ** np.maximum(diff, 0), 0.0) * DH ** -0.5
    decay = np.ascontiguousarray(decay.transpose(1, 0, 2).reshape(P, H * P), dtype=f32)
    inv = (1.0 / f32(10000.0) ** (np.arange(0, DH, 2, dtype=f32) / f32(DH))).astype(f32)
    freqs = np.arange(S, dtype=f32)[:, None] * inv[None, :]
    cos, sin = np.cos(freqs), np.sin(freqs)
    rope = np.stack([np.tile(np.concatenate([cos, cos], 1), (1, H)),
                     np.tile(np.concatenate([-sin, sin], 1), (1, H))]).astype(f32)
    rope = np.ascontiguousarray(rope.reshape(2, NCH, P, P).transpose(2, 0, 1, 3))
    sel = np.zeros((P, E * P + P), f32)
    for part in range(3):
        for e in range(E):
            sel[part * E + e, e * P:(e + 1) * P] = 1.0
    sel[:, E * P:] = np.eye(P)
    return const, decay, rope, sel


def down_rows(w, chunks):
    e, f, d = w.shape
    full = np.zeros((e, chunks * P, d), w.dtype)
    full[:, :f] = w
    return full.reshape(e, chunks, P, d).transpose(0, 2, 1, 3).reshape(e, P, chunks * d)


def kernel(**inputs):
    import concourse.bacc as bacc
    from concourse.bass_utils import run_bass_kernel_spmd

    a = {k: np.asarray(v) for k, v in inputs.items()}
    x = np.ascontiguousarray(a["L0_attn_x"].reshape(T, P).T)
    w0 = np.concatenate([a["L0_ffn_Wg"], a["L0_ffn_Wu"], down_rows(a["L0_ffn_Wd"], CH[0])], axis=2)
    w1 = np.concatenate([a["L1_ffn_we1"], down_rows(a["L1_ffn_we2"], CH[1])], axis=2)
    column = lambda v: v.reshape(P, 1)
    spread = lambda v: np.broadcast_to(np.tile(v, NT)[None, :], (P, NT * E))
    vectors = np.concatenate(
        [column(a[f"L0_attn_time_mix_{c}"]) for c in "kvr"]
        + [column(a["L0_attn_time_decay"]), column(a["L0_attn_time_first"]), column(a["L1_ffn_rb1"]),
           a["L1_ffn_be1"].reshape(NCK[1], P).T, a["L1_ffn_be2"].T, a["L0_ffn_Ws"], a["L1_ffn_rw2"],
           spread(a["L0_ffn_bs"]), spread(a["L1_ffn_rb2"])], axis=1)
    swapped = np.arange(P).reshape(H, 2, DH // 2)[:, ::-1].ravel()
    wq, wk = a["L1_attn_Wq"], a["L1_attn_Wk"]
    square = np.concatenate(
        [a["L0_attn_Wk"].T, a["L0_attn_Wv"].T, a["L0_attn_Wr"].T, a["L0_attn_Wo"].T,
         wq.T, wk.T, wq[swapped].T, wk[swapped].T, a["L1_attn_Wv"].T, a["L1_attn_Wg"].T, a["L1_attn_Wo"].T,
         a["L1_ffn_rw1"]], axis=1)
    gn = np.concatenate([np.broadcast_to(a[n][None, :], (P, P)) for n in ("L1_attn_gn_w", "L1_attn_gn_b")], axis=1)
    const, decay, rope, sel = constants()
    arrays = {"x": x, "w0": w0, "w1": w1, "vectors": vectors, "square": square, "gn": gn, "const": const, "sel": sel,
              "rope": rope, "decay": decay}
    arrays = {f"in_{k}": np.ascontiguousarray(v) for k, v in arrays.items()}

    nc = bacc.Bacc("TRN2", target_bir_lowering=False, num_devices=1)
    aps = [nc.dram_tensor(k, v.shape, mybir.dt.from_np(v.dtype), kind="ExternalInput").ap() for k, v in arrays.items()]
    out = nc.dram_tensor("out", (P, T), F32, kind="ExternalOutput").ap()
    build_block(nc, *aps, out)
    res = run_bass_kernel_spmd(nc, [arrays], core_ids=[0])
    return np.ascontiguousarray(res.results[0]["out"].T).reshape(NB, S, P)
```
